# Optimizing a Trainium2 kernel written in Bass

```python
import numpy as np
import jax
import jax.numpy as jnp

def _softmax(x, axis=-1):
    return jax.nn.softmax(x, axis=axis)

def _gelu(x):
    return jax.nn.gelu(x, approximate=True)

def _silu(x):
    return jax.nn.silu(x)

def _sigmoid(x):
    return jax.nn.sigmoid(x)

def _layernorm(x, axis=-1, eps=1e-05):
    m = jnp.mean(x, axis=axis, keepdims=True)
    v = jnp.var(x, axis=axis, keepdims=True)
    return (x - m) / jnp.sqrt(v + eps)

def _scatter_add(tgt, idx, src, axis=0):
    return tgt.at[idx].add(src)

def _segment_sum(src, seg, n):
    return jax.ops.segment_sum(src, seg, n)
kernel_name = 'mk_gnn_resnorm_d2_gnn_r64_17543c'

def setup_inputs(seed: int=0):
    np.random.seed(seed)
    _w = jnp.asarray

    def _rec_inputs():
        import jax
        import jax.numpy as jnp
        _gk = jax.random.key(seed)
        x = -0.0003713 + 1 * jax.random.normal(jax.random.fold_in(_gk, 1), (50000, 256), jnp.float32)
        src = jax.random.randint(jax.random.fold_in(_gk, 2), (25000,), 0, 50000, jnp.int32)
        dst = jax.random.randint(jax.random.fold_in(_gk, 3), (25000,), 0, 50000, jnp.int32)
        _o = jnp.argsort(dst, stable=True)
        src = src[_o]
        dst = dst[_o]
        edge_attr_3 = 0.000669165 + 0.999965 * jax.random.normal(jax.random.fold_in(_gk, 11), (25000, 3), jnp.float32)
        return (x, src, dst, edge_attr_3)
    x, src, dst, edge_attr_3 = _rec_inputs()

    def _L0_gnn_setup():
        import jax, jax.numpy as jnp
        import numpy as np
        N_NODES, IN_DIM, HID, OUT_DIM, H, E = (50000, 256, 256, 256, 8, 6250)
        NEG_SLOPE = 0.2
        LN_EPS = 1e-05
        key = jax.random.key(seed)
        ks = jax.random.split(key, 8)
        s = 1.0 / np.sqrt(IN_DIM)
        return {'x': jax.random.normal(ks[0], (N_NODES, IN_DIM), jnp.float32), 'edge_index': jax.random.randint(ks[1], (2, E), 0, N_NODES, jnp.int64), 'W': jax.random.normal(ks[2], (H, IN_DIM, HID), jnp.float32) * s, 'att_src': jax.random.normal(ks[3], (H, HID), jnp.float32) * s, 'att_dst': jax.random.normal(ks[4], (H, HID), jnp.float32) * s, 'bias_gat': jnp.zeros((H, HID), jnp.float32), 'gate_weights': jnp.ones((H,), jnp.float32) / H, 'ln_gamma': jnp.ones((HID,), jnp.float32), 'ln_beta': jnp.zeros((HID,), jnp.float32), 'Wo': jax.random.normal(ks[5], (OUT_DIM, HID), jnp.float32) * (1.0 / np.sqrt(HID)), 'bo': jnp.zeros((OUT_DIM,), jnp.float32)}
    _L0_gnn_all = _L0_gnn_setup()
    _L0_gnn_in = {k: v for k, v in _L0_gnn_all.items() if k in ('W', 'att_src', 'att_dst', 'bias_gat', 'gate_weights', 'ln_gamma', 'ln_beta', 'Wo', 'bo')}
    del _L0_gnn_all

    def _L1_gnn_setup():
        import jax, jax.numpy as jnp
        import numpy as np
        N_NODES = 50000
        N_EDGES = 12500
        HID = 256
        EDGE_DIM = 3
        key = jax.random.key(seed)
        ks = jax.random.split(key, 10)
        h = jax.random.normal(ks[0], (N_NODES, HID), dtype=jnp.float32)
        edge_index = jax.random.randint(ks[1], (2, N_EDGES), 0, N_NODES, dtype=jnp.int64)
        edge_attr = jax.random.normal(ks[2], (N_EDGES, EDGE_DIM), dtype=jnp.float32)
        half = HID // 2
        W1 = jax.random.normal(ks[3], (EDGE_DIM, half), dtype=jnp.float32) / np.sqrt(EDGE_DIM)
        b1 = jnp.zeros((half,), dtype=jnp.float32)
        W2 = jax.random.normal(ks[4], (half, 1), dtype=jnp.float32) / np.sqrt(half)
        b2 = jnp.zeros((1,), dtype=jnp.float32)
        Wc = jax.random.normal(ks[5], (HID, HID), dtype=jnp.float32) / np.sqrt(HID)
        bc = jnp.zeros((HID,), dtype=jnp.float32)
        return {'h': h, 'edge_index': edge_index, 'edge_attr': edge_attr, 'W1': W1, 'b1': b1, 'W2': W2, 'b2': b2, 'Wc': Wc, 'bc': bc}
    _L1_gnn_all = _L1_gnn_setup()
    _L1_gnn_in = {k: v for k, v in _L1_gnn_all.items() if k in ('W1', 'b1', 'W2', 'b2', 'Wc', 'bc')}
    del _L1_gnn_all
    return {'x': x, 'src': src, 'dst': dst, 'edge_attr_3': edge_attr_3, 'L0_gnn_W': _L0_gnn_in['W'], 'L0_gnn_att_src': _L0_gnn_in['att_src'], 'L0_gnn_att_dst': _L0_gnn_in['att_dst'], 'L0_gnn_bias_gat': _L0_gnn_in['bias_gat'], 'L0_gnn_gate_weights': _L0_gnn_in['gate_weights'], 'L0_gnn_ln_gamma': _L0_gnn_in['ln_gamma'], 'L0_gnn_ln_beta': _L0_gnn_in['ln_beta'], 'L0_gnn_Wo': _L0_gnn_in['Wo'], 'L0_gnn_bo': _L0_gnn_in['bo'], 'L1_gnn_W1': _L1_gnn_in['W1'], 'L1_gnn_b1': _L1_gnn_in['b1'], 'L1_gnn_W2': _L1_gnn_in['W2'], 'L1_gnn_b2': _L1_gnn_in['b2'], 'L1_gnn_Wc': _L1_gnn_in['Wc'], 'L1_gnn_bc': _L1_gnn_in['bc']}

def reference(x, src, dst, edge_attr_3, L0_gnn_W, L0_gnn_att_src, L0_gnn_att_dst, L0_gnn_bias_gat, L0_gnn_gate_weights, L0_gnn_ln_gamma, L0_gnn_ln_beta, L0_gnn_Wo, L0_gnn_bo, L1_gnn_W1, L1_gnn_b1, L1_gnn_W2, L1_gnn_b2, L1_gnn_Wc, L1_gnn_bc):
    import jax
    import jax.numpy as jnp

    def _L0_gnn_ref(x, edge_index, W, att_src, att_dst, bias_gat, gate_weights, ln_gamma, ln_beta, Wo, bo):
        import jax, jax.numpy as jnp
        import numpy as np
        N_NODES, IN_DIM, HID, OUT_DIM, H, E = (50000, 256, 256, 256, 8, 6250)
        NEG_SLOPE = 0.2
        LN_EPS = 1e-05
        N = x.shape[0]
        D = W.shape[2]
        loops = jnp.arange(N, dtype=edge_index.dtype)
        src = jnp.concatenate([edge_index[0], loops])
        dst = jnp.concatenate([edge_index[1], loops])
        h = jnp.einsum('nf,hfd->hnd', x, W)
        a_s = jnp.einsum('hnd,hd->hn', h, att_src)
        a_d = jnp.einsum('hnd,hd->hn', h, att_dst)
        e = jax.nn.leaky_relu(a_s[:, src] + a_d[:, dst], NEG_SLOPE)
        gw = jax.nn.softmax(gate_weights)

        def head_step(acc, xs):
            h_h, e_h, g_h = xs
            m = jax.ops.segment_max(e_h, dst, num_segments=N)
            ex = jnp.exp(e_h - m[dst])
            den = jax.ops.segment_sum(ex, dst, num_segments=N)
            alpha = ex / den[dst]
            out = jax.ops.segment_sum(h_h[src] * alpha[:, None], dst, num_segments=N)
            return (acc + g_h * out, None)
        agg, _ = jax.lax.scan(head_step, jnp.zeros((N, D), x.dtype), (h, e, gw))
        agg = agg + gw @ bias_gat
        res = agg + x[:, :D]
        mu = jnp.mean(res, axis=-1, keepdims=True)
        var = jnp.var(res, axis=-1, keepdims=True)
        ln = ln_gamma * (res - mu) * jax.lax.rsqrt(var + LN_EPS) + ln_beta
        return ln @ Wo.T + bo

    def _L1_gnn_ref(h, edge_index, edge_attr, W1, b1, W2, b2, Wc, bc):
        import jax, jax.numpy as jnp
        import numpy as np
        N_NODES = 50000
        N_EDGES = 12500
        HID = 256
        EDGE_DIM = 3
        N = h.shape[0]
        t = jax.nn.silu(edge_attr @ W1 + b1)
        w = jax.nn.sigmoid((t @ W2 + b2)[:, 0])
        loop = jnp.arange(N, dtype=edge_index.dtype)
        row = jnp.concatenate([edge_index[0], loop])
        col = jnp.concatenate([edge_index[1], loop])
        ew = jnp.concatenate([w, jnp.ones((N,), dtype=w.dtype)])
        deg = jax.ops.segment_sum(ew, col, num_segments=N)
        dinv = jnp.where(deg > 0, jax.lax.rsqrt(deg), 0.0)
        norm = dinv[row] * ew * dinv[col]
        x = h @ Wc
        msg = x[row] * norm[:, None]
        out = jax.ops.segment_sum(msg, col, num_segments=N) + bc
        return out
    edge_index = jnp.stack([src, dst])
    x = _layernorm(x + _L0_gnn_ref(x, edge_index, L0_gnn_W, L0_gnn_att_src, L0_gnn_att_dst, L0_gnn_bias_gat, L0_gnn_gate_weights, L0_gnn_ln_gamma, L0_gnn_ln_beta, L0_gnn_Wo, L0_gnn_bo), axis=-1)
    x = _layernorm(x + _L1_gnn_ref(x, edge_index, edge_attr_3, L1_gnn_W1, L1_gnn_b1, L1_gnn_W2, L1_gnn_b2, L1_gnn_Wc, L1_gnn_bc), axis=-1)
    return x

_drawn_inputs = setup_inputs


def setup_inputs(seed=0):
    import zlib

    import numpy as np

    out = dict(_drawn_inputs(seed))
    spreads = {'L0_gnn_bias_gat': (0.0, 0.317),
     'L0_gnn_gate_weights': (0.125, 0.6),
     'L0_gnn_ln_gamma': (1.0, 0.2),
     'L0_gnn_ln_beta': (0.0, 0.1),
     'L0_gnn_bo': (0.0, 0.1),
     'L1_gnn_b1': (0.0, 0.8),
     'L1_gnn_bc': (0.0, 0.1)}
    factors = {'L0_gnn_att_dst': 4.513}
    for name, (base, spread) in spreads.items():
        noise = np.random.default_rng([zlib.crc32(name.encode()), seed]).standard_normal(out[name].shape)
        drawn = base * np.exp(spread * noise) if base else spread * noise
        out[name] = jnp.asarray(drawn.astype(out[name].dtype))
    for name, factor in factors.items():
        out[name] = (out[name] * factor).astype(out[name].dtype)
    return out
```

```python
from contextlib import ExitStack

import numpy as np
import concourse.bass as bass
from concourse import mybir

FP32 = mybir.dt.float32
FP32R = mybir.dt.float32r
BF16 = mybir.dt.bfloat16
I32 = mybir.dt.int32
ALU = mybir.AluOpType
ACT = mybir.ActivationFunctionType
AX = mybir.AxisListType

P = 128
N = 50000
E = 25000
D = 256
A = D // P
H = 8
TB = 4
BLK = TB * P
EB = -(-E // BLK)
EP = EB * BLK
ET = EP // P
NB = 2 * -(-N // (2 * BLK))
NT = NB * TB
K = 14
C = EP // K
CT = C // P
SP_ROWS = H * K
RP = SP_ROWS + K
ROW = D + 4
BIG = 1 << 20
HUGE = 1.0e30
SLOPE = 0.2
EPS = 1.0e-5
LAST_BASE = N - BLK


def pipeline(eng, units, unroll, depth, steps):
    most = max(lag for lag, _ in steps)
    head = unroll * (-(-(most + depth) // unroll))
    whole = units // unroll * unroll

    def peeled(turn):
        for lag, fn in steps:
            g = turn - lag
            if 0 <= g < units:
                fn(g, g % unroll, g // unroll)

    for turn in range(head):
        peeled(turn)
    with eng.Fori(head // unroll, whole // unroll) as j:
        for r in range(unroll):
            for lag, fn in steps:
                fn(j * unroll + (r - lag), (r - lag) % unroll, j + (r - lag) // unroll)
    for turn in range(whole, units + most):
        peeled(turn)


def wait_reuse(eng, sem, count):
    if not isinstance(count, int) or count > 0:
        eng.wait_ge(sem, count)


def hold(eng, sem, count, gate):
    if not isinstance(count, int):
        eng.wait_ge(sem, count)
        eng.sem_inc(gate, 1)
    elif count > 0:
        eng.wait_ge(sem, count)


def build(nc, x, edge_index_cols, edge_dst_cols, edge_next_cols, dst_ext, edge_attr_t,
          W, att_src, att_dst, bias_gat, gate_weights, gamma_cols, beta_cols, Wo, bo,
          W1, b1, W2, b2, Wc, bc, out, dbg=None):
    diff_t = nc.dram_tensor("diff_t", (EB, P, A * BLK), FP32).ap()
    scores = nc.dram_tensor("scores", (2 * H, EP), FP32).ap()
    edge_pre = nc.dram_tensor("edge_pre", (1, EP), FP32).ap()
    same_row = nc.dram_tensor("same_row", (K, C), BF16).ap()
    last_of = nc.dram_tensor("last_of", (N, 1), I32).ap()
    gat_tab = nc.dram_tensor("gat_tab", (EP, ROW), FP32).ap()
    x1_tab = nc.dram_tensor("x1_tab", (N, ROW), FP32).ap()
    gcn_tab = nc.dram_tensor("gcn_tab", (EP, ROW), FP32).ap()

    ctx = ExitStack()
    with ctx:
        def sb(name, shape, dt=FP32, stack=ctx):
            return stack.enter_context(nc.sbuf_tensor(name, shape, dt))

        def sem(name):
            return ctx.enter_context(nc.semaphore(name))

        bank = [ctx.enter_context(nc.psum_tensor(f"bank{i}", [P, 512], FP32)) for i in range(8)]

        ident = sb("ident", [P, P])
        one = sb("one", [1, 1])
        eps_col = sb("eps_col", [P, 1])
        w_hi = sb("w_hi", [P, A, H * D], FP32R)
        w_lo = sb("w_lo", [P, A, H * D], FP32R)
        m1 = sb("m1", [P, A, D])
        cwo = sb("cwo", [P, A, D])
        wc = sb("wc", [P, A, D])
        bgat = sb("bgat", [P, D])
        out_bias = sb("out_bias", [P, D])
        bc_row = sb("bc_row", [P, D])
        v_diff = sb("v_diff", [P, A, 2 * H])
        v_dst = sb("v_dst", [P, A, 2 * H])
        w1_sb = sb("w1_sb", [3, P])
        b1_col = sb("b1_col", [P, 1])
        w2_col = sb("w2_col", [P, 1])
        b2_one = sb("b2_one", [1, 1])
        gate_bc = sb("gate_bc", [P, H])
        gate_rows = sb("gate_rows", [P, 1])
        idx_cols = sb("idx_cols", [P, EB, 2 * TB], I32)
        beta_cols_sb = sb("beta_cols_sb", [P, H + 1, ET])
        deg_inv = sb("deg_inv", [P, ET])
        dinv = sb("dinv", [P, ET])
        scatter_to = sb("scatter_to", [P, ET], I32)
        edge_ids = sb("edge_ids", [P, ET], I32)

        sp_gate = sem("sp_gate")
        pool_gate = sem("pool_gate")
        dve_gate = sem("dve_gate")

        s_load = sem("s_load")
        s_const = sem("s_const")
        s_prep = sem("s_prep")
        s_wot = sem("s_wot")
        s_wot_sb = sem("s_wot_sb")
        s_beta_sb = sem("s_beta_sb")
        s_bout = sem("s_bout")
        s_wg = sem("s_wg")
        s_mean = sem("s_mean")
        s_split = sem("s_split")
        s_hi = sem("s_hi")
        s_gexp_in = sem("s_gexp_in")
        s_gexp = sem("s_gexp")
        s_noedge = sem("s_noedge")
        s_nostore = sem("s_nostore")
        with ExitStack() as prep:
            w_sb = sb("w_sb", [P, A, H * D], stack=prep)
            att_bc = sb("att_bc", [P, 2, H * D], stack=prep)
            prod = sb("prod", [P, H * D], stack=prep)
            bias_bc = sb("bias_bc", [P, H * D], stack=prep)
            wo_sb = sb("wo_sb", [P, A, D], stack=prep)
            wot = sb("wot", [P, A, D], stack=prep)
            wg = sb("wg", [P, A, D], stack=prep)
            gam = sb("gam", [P, A], stack=prep)
            bet = sb("bet", [P, A], stack=prep)
            bet_bc = sb("bet_bc", [P, A, P], stack=prep)
            ones = sb("ones", [P, P], stack=prep)
            mean_m = sb("mean_m", [P, P], stack=prep)
            bo_row = sb("bo_row", [P, D], stack=prep)
            gmax = sb("gmax", [P, 1], stack=prep)
            gsh = sb("gsh", [P, H + 1], stack=prep)
            gexp = sb("gexp", [P, H + 1], stack=prep)
            gsum = sb("gsum", [P, 1], stack=prep)
            vtmp = sb("vtmp", [P, 2, A, H], stack=prep)
            none_yet = sb("none_yet", [80, N // 80], I32, stack=prep)
            dst_c = sb("dst_c", [P, ET], I32, stack=prep)
            nxt_c = sb("nxt_c", [P, ET], I32, stack=prep)
            more = sb("more", [P, ET], FP32, stack=prep)

            loads = []
            for a in range(A):
                loads.append((w_sb[:, a, :].rearrange("p (h d) -> p h d", h=H),
                              W[:, a * P:(a + 1) * P, :].rearrange("h p d -> p h d")))
            loads += [
                (att_bc[:, 0, :], att_src.rearrange("h d -> (h d)").partition_broadcast(P)),
                (att_bc[:, 1, :], att_dst.rearrange("h d -> (h d)").partition_broadcast(P)),
                (bias_bc[:, :], bias_gat.rearrange("h d -> (h d)").partition_broadcast(P)),
                (gate_bc[:, :], gate_weights.partition_broadcast(P)),
                (wo_sb[:, :, :], Wo.rearrange("(a p) k -> p a k", p=P)),
                (wc[:, :, :], Wc.rearrange("(a p) k -> p a k", p=P)),
                (gam[:, :], gamma_cols), (bet[:, :], beta_cols),
                (bo_row[:, :], bo.partition_broadcast(P)),
                (bc_row[:, :], bc.partition_broadcast(P)),
                (w1_sb[:, :], W1), (b1_col[:, :], b1.rearrange("(p o) -> p o", o=1)),
                (w2_col[:, :], W2), (b2_one[:, :], b2.rearrange("(p o) -> p o", o=1)),
                (idx_cols[:, :, :], edge_index_cols.rearrange("p (b c) -> p b c", b=EB)),
                (dst_c[:, :], edge_dst_cols), (nxt_c[:, :], edge_next_cols),
            ]
            for h in range(H):
                loads.append((gate_rows[h * K:(h + 1) * K, :], gate_weights[h:h + 1].partition_broadcast(K)))
            n_loads = 16 * len(loads)

            with nc.Block() as block:
                @block.sync
                def _(sp):
                    for to, of in loads[::2]:
                        sp.dma_start(to, of).then_inc(s_load, 16)
                    hold(sp, s_noedge, 1, sp_gate)
                    sp.dma_start(last_of.rearrange("(p c) o -> p (c o)", p=80), none_yet[:, :]).then_inc(s_nostore, 16)
                    hold(sp, s_nostore, 16, sp_gate)

                @block.gpsimd
                def _(pool):
                    nc.gpsimd.memset(none_yet[:, :], BIG).then_inc(s_noedge, 1)
                    nc.gpsimd.memset(ident[:, :], 0.0).then_inc(s_const, 1)
                    nc.gpsimd.memset(one[:, :], 1.0).then_inc(s_const, 1)
                    nc.gpsimd.memset(eps_col[:, :], EPS).then_inc(s_const, 1)
                    nc.gpsimd.memset(ones[:, :], 1.0).then_inc(s_const, 1)
                    nc.gpsimd.memset(mean_m[:, :], 1.0 / D).then_inc(s_const, 1)
                    hold(pool, s_const, 5, pool_gate)
                    nc.gpsimd.affine_select(out=ident[:, :], in_=ident[:, :], compare_op=ALU.not_equal, fill=1.0,
                                            base=0, pattern=[[-1, P]], channel_multiplier=1).then_inc(s_const, 1)
                    nc.gpsimd.iota(edge_ids[:, :], pattern=[[P, ET]], base=0, channel_multiplier=1).then_inc(s_const, 1)

                @block.scalar
                def _(act):
                    for to, of in loads[1::2]:
                        act.dma_start(to, of).then_inc(s_load, 16)
                    act.wait_ge(s_load, n_loads)
                    nc.scalar.activation(w_hi[:, :, :], w_sb[:, :, :], ACT.Copy).then_inc(s_hi, 1)
                    act.wait_ge(s_gexp_in, 1)
                    nc.scalar.activation(gexp[:, :], gsh[:, :], ACT.Exp).then_inc(s_gexp, 1)

                @block.vector
                def _(dve):
                    done = [0]

                    def link(ins):
                        done[0] += 1
                        ins.then_inc(s_prep, 1)
                        dve.wait_ge(s_prep, done[0])

                    dve.wait_ge(s_load, n_loads)
                    link(nc.vector.reduce_max(gmax[:, :], gate_bc[:, :], AX.X))
                    link(nc.vector.memset(gsh[:, :], 0.0))
                    link(nc.vector.tensor_scalar(gsh[:, 0:H], gate_bc[:, :], gmax[:, 0:1], None, ALU.subtract))
                    nc.vector.tensor_scalar(gsh[0:SP_ROWS, H:H + 1], gate_rows[0:SP_ROWS, :], gmax[0:SP_ROWS, 0:1], None,
                                            ALU.subtract).then_inc(s_gexp_in, 1)
                    dve.wait_ge(s_gexp, 1)
                    link(nc.vector.reduce_sum(gsum[:, :], gexp[:, 0:H], AX.X))
                    link(nc.vector.reciprocal(gmax[:, :], gsum[:, :]))
                    link(nc.vector.tensor_scalar(gate_bc[:, :], gexp[:, 0:H], gmax[:, 0:1], None, ALU.mult))
                    link(nc.vector.memset(gate_rows[:, :], 1.0))
                    link(nc.vector.tensor_scalar(gate_rows[0:SP_ROWS, :], gexp[0:SP_ROWS, H:H + 1], gmax[0:SP_ROWS, 0:1],
                                                 None, ALU.mult))
                    for h in range(H):
                        wh = w_sb[:, :, h * D:(h + 1) * D]
                        bh = bias_bc[:, h * D:(h + 1) * D]
                        g = gate_bc[:, h:h + 1]
                        if h == 0:
                            link(nc.vector.tensor_scalar(m1[:, :, :], wh, g, None, ALU.mult))
                            link(nc.vector.tensor_scalar(bgat[:, :], bh, g, None, ALU.mult))
                        else:
                            link(nc.vector.scalar_tensor_tensor(m1[:, :, :], wh, g, m1[:, :, :], ALU.mult, ALU.add))
                            link(nc.vector.scalar_tensor_tensor(bgat[:, :], bh, g, bgat[:, :], ALU.mult, ALU.add))
                    dve.wait_ge(s_const, 7)
                    for a in range(A):
                        link(nc.vector.tensor_tensor(m1[:, a, a * P:(a + 1) * P], m1[:, a, a * P:(a + 1) * P],
                                                     ident[:, :], ALU.add))
                    for s in range(2):
                        for a in range(A):
                            link(nc.vector.tensor_tensor(prod[:, :], w_sb[:, a, :], att_bc[:, s, :], ALU.mult))
                            link(nc.vector.reduce_sum(vtmp[:, s, a, :], prod[:, :].rearrange("p (h d) -> p h d", h=H), AX.X))
                    link(nc.vector.memset(v_diff[:, :, :], 0.0))
                    link(nc.vector.tensor_copy(v_diff[:, :, H:2 * H], vtmp[:, 0, :, :]))
                    for c in range(2):
                        link(nc.vector.tensor_tensor(v_dst[:, :, c * H:(c + 1) * H], vtmp[:, 0, :, :], vtmp[:, 1, :, :], ALU.add))
                    dve.wait_ge(s_wot, 2 * A)
                    for a in range(A):
                        link(nc.vector.tensor_copy(wot[:, a, :], bank[a][:, 0:D]))
                    for a in range(A):
                        link(nc.vector.tensor_scalar(wg[:, a, :], wot[:, a, :], gam[:, a:a + 1], None, ALU.mult))
                        link(nc.vector.tensor_scalar(bet_bc[:, a, :], ones[:, :], bet[:, a:a + 1], None, ALU.mult))
                    nc.vector.tensor_copy(more[:, 0:1], gam[:, 0:1]).then_inc(s_wg, 1)
                    dve.wait_ge(s_mean, 1)
                    for a in range(A):
                        link(nc.vector.tensor_tensor(cwo[:, a, :], wg[:, a, :], bank[2][:, 0:D], ALU.subtract))
                    link(nc.vector.tensor_tensor(out_bias[:, :], bo_row[:, :], bank[3][:, 0:D], ALU.add))
                    link(nc.vector.tensor_tensor(more[:, :], dst_c[:, :], nxt_c[:, :], ALU.is_equal))
                    link(nc.vector.scalar_tensor_tensor(scatter_to[:, :], more[:, :], float(BIG), dst_c[:, :],
                                                        ALU.mult, ALU.add))
                    dve.wait_ge(s_hi, 1)
                    link(nc.vector.tensor_tensor(w_lo[:, :, :], w_sb[:, :, :], w_hi[:, :, :].bitcast(FP32), ALU.subtract))

                @block.tensor
                def _(pe):
                    pe.wait_ge(s_load, n_loads)
                    pe.wait_ge(s_const, 7)
                    for ob in range(A):
                        for kb in range(A):
                            nc.tensor.transpose(bank[kb][:, ob * P:(ob + 1) * P], wo_sb[:, ob, kb * P:(kb + 1) * P],
                                                ident[:, :]).then_inc(s_wot, 1)
                    pe.wait_ge(s_wg, 1)
                    for a in range(A):
                        nc.tensor.matmul(bank[2][:, 0:D], mean_m[:, :], wg[:, a, :], start=a == 0, stop=a == A - 1)
                    for a in range(A):
                        last = nc.tensor.matmul(bank[3][:, 0:D], bet_bc[:, a, :], wot[:, a, :], start=a == 0, stop=a == A - 1)
                    last.then_inc(s_mean, 1)

        a_idx = sem("a_idx")
        a_rows = [sem(f"a_rows{s}") for s in range(2)]
        a_attr = [sem(f"a_attr{s}") for s in range(2)]
        a_diff = sem("a_diff")
        a_dps = sem("a_dps")
        a_xps = sem("a_xps")
        a_dsb = sem("a_dsb")
        a_xsb = sem("a_xsb")
        a_zps = sem("a_zps")
        a_tsb = sem("a_tsb")
        a_sps = sem("a_sps")
        a_wps = sem("a_wps")
        a_ssb = sem("a_ssb")
        a_lrelu = sem("a_lrelu")
        a_out = [sem(f"a_out{s}") for s in range(2)]
        with ExitStack() as ph:
            idx = sb("idx", [P, 2, 2 * TB], I32, stack=ph)
            xs = sb("xs", [P, 2, TB, D], stack=ph)
            xd = sb("xd", [P, 2, TB, D], stack=ph)
            df = sb("df", [P, 2, TB, D], stack=ph)
            d_t = sb("d_t", [P, 2, A, BLK], stack=ph)
            x_t = sb("x_t", [P, 2, A, BLK], stack=ph)
            attr = sb("attr", [3, 2, BLK], stack=ph)
            hid = sb("hid", [P, 2, BLK], stack=ph)
            sc = sb("sc", [2 * H, 2, BLK], stack=ph)
            pre = sb("pre", [1, 2, BLK], stack=ph)

            with nc.Block() as block:
                @block.gpsimd
                def _(pool):
                    def gather(b, s, q):
                        hold(pool, a_diff, b - 1, pool_gate)
                        hold(pool, a_xps, b - 1, pool_gate)
                        nc.gpsimd.tensor_copy(idx[:, s, :], idx_cols[:, bass.ds(b, 1), :].rearrange("p o c -> p (o c)")
                                              ).then_inc(a_idx, 1)
                        hold(pool, a_idx, b + 1, pool_gate)
                        for t in range(TB):
                            for rows, c in ((xs, t), (xd, TB + t)):
                                nc.gpsimd.indirect_dma_start(
                                    out=rows[:, s, t, :], out_offset=None, in_=x[:, :],
                                    in_offset=bass.IndirectOffsetOnAxis(ap=idx[:, s, c:c + 1], axis=0),
                                    bounds_check=N - 1, oob_is_err=False).then_inc(a_rows[s], 16)
                    pipeline(pool, EB, 2, 2, [(0, gather)])

                @block.sync
                def _(sp):
                    def load_attr(b, s, q):
                        hold(sp, a_zps, b - 1, sp_gate)
                        sp.dma_start(attr[:, s, :], edge_attr_t[:, bass.ds(b * BLK, BLK)]).then_inc(a_attr[s], 16)

                    def store(b, s, q):
                        hold(sp, a_dsb, b + 1, sp_gate)
                        sp.dma_start(diff_t[bass.ds(b, 1), :, :].rearrange("o p c -> (o p) c"),
                                     d_t[:, s, :, :].rearrange("p a e -> p (a e)")).then_inc(a_out[s], 16)
                        hold(sp, a_ssb, b + 1, sp_gate)
                        sp.dma_start(scores[:, bass.ds(b * BLK, BLK)], sc[:, s, :]).then_inc(a_out[s], 16)
                        sp.dma_start(edge_pre[:, bass.ds(b * BLK, BLK)], pre[:, s, :]).then_inc(a_out[s], 16)
                    pipeline(sp, EB, 2, 2, [(0, load_attr), (1, store)])
                    hold(sp, a_out[0], 48 * ((EB + 1) // 2), sp_gate)
                    hold(sp, a_out[1], 48 * (EB // 2), sp_gate)

                @block.vector
                def _(dve):
                    def diff(b, s, q):
                        dve.wait_ge(a_rows[s], 16 * 2 * TB * (q + 1))
                        wait_reuse(dve, a_dps, b - 1)
                        nc.vector.tensor_tensor(df[:, s, :, :], xs[:, s, :, :], xd[:, s, :, :], ALU.subtract
                                                ).then_inc(a_diff, 1)

                    def evacuate(b, s, q):
                        dve.wait_ge(a_sps, b + 1)
                        dve.wait_ge(a_wps, b + 1)
                        wait_reuse(dve, a_out[s], 48 * q)
                        nc.vector.tensor_scalar(sc[:, s, :], bank[5][0:2 * H, :], SLOPE, None, ALU.mult).then_inc(a_lrelu, 1)
                        dve.wait_ge(a_lrelu, b + 1)
                        nc.vector.tensor_tensor(sc[:, s, :], sc[:, s, :], bank[5][0:2 * H, :], ALU.max)
                        nc.vector.tensor_scalar(pre[:, s, :], bank[6][0:1, :], b2_one[0:1, 0:1], None, ALU.add
                                                ).then_inc(a_ssb, 1)
                    pipeline(dve, EB, 2, 2, [(0, diff), (1, evacuate)])

                @block.tensor
                def _(pe):
                    def turn(b, s, q):
                        pe.wait_ge(a_diff, b + 1)
                        wait_reuse(pe, a_dsb, b)
                        for t in range(TB):
                            for a in range(A):
                                last = nc.tensor.transpose(bank[a][:, t * P:(t + 1) * P],
                                                           df[:, s, t, a * P:(a + 1) * P], ident[:, :])
                        last.then_inc(a_dps, 1)
                        wait_reuse(pe, a_xsb, b)
                        for t in range(TB):
                            for a in range(A):
                                last = nc.tensor.transpose(bank[2 + a][:, t * P:(t + 1) * P],
                                                           xd[:, s, t, a * P:(a + 1) * P], ident[:, :])
                        last.then_inc(a_xps, 1)
                        pe.wait_ge(a_attr[s], 16 * (q + 1))
                        wait_reuse(pe, a_tsb, b)
                        nc.tensor.matmul(bank[4][:, :], w1_sb[:, :], attr[:, s, :], start=True, stop=True).then_inc(a_zps, 1)

                    def score(b, s, q):
                        pe.wait_ge(a_dsb, b + 1)
                        pe.wait_ge(a_xsb, b + 1)
                        wait_reuse(pe, a_ssb, b)
                        for a in range(A):
                            nc.tensor.matmul(bank[5][0:2 * H, :], v_diff[:, a, :], d_t[:, s, a, :], start=a == 0, stop=False)
                        for a in range(A):
                            last = nc.tensor.matmul(bank[5][0:2 * H, :], v_dst[:, a, :], x_t[:, s, a, :], start=False, stop=a == A - 1)
                        last.then_inc(a_sps, 1)
                        pe.wait_ge(a_tsb, b + 1)
                        nc.tensor.matmul(bank[6][0:1, :], w2_col[:, :], hid[:, s, :], start=True, stop=True).then_inc(a_wps, 1)
                    pipeline(pe, EB, 2, 2, [(0, turn), (1, score)])

                @block.scalar
                def _(act):
                    def evacuate(b, s, q):
                        act.wait_ge(a_dps, b + 1)
                        wait_reuse(act, a_out[s], 48 * q)
                        wait_reuse(act, a_sps, b - 1)
                        nc.scalar.activation(d_t[:, s, 0, :], bank[0][:, :], ACT.Copy)
                        nc.scalar.activation(d_t[:, s, 1, :], bank[1][:, :], ACT.Copy).then_inc(a_dsb, 1)
                        act.wait_ge(a_xps, b + 1)
                        nc.scalar.activation(x_t[:, s, 0, :], bank[2][:, :], ACT.Copy)
                        nc.scalar.activation(x_t[:, s, 1, :], bank[3][:, :], ACT.Copy).then_inc(a_xsb, 1)
                        act.wait_ge(a_zps, b + 1)
                        wait_reuse(act, a_wps, b - 1)
                        nc.scalar.activation(hid[:, s, :], bank[4][:, :], ACT.Silu, bias=b1_col[:, 0:1]).then_inc(a_tsb, 1)
                    pipeline(act, EB, 2, 2, [(0, evacuate)])

        s_seg_load = sem("s_seg_load")
        s_score_load = sem("s_score_load")
        s_zeroed = sem("s_zeroed")
        s_dve = sem("s_dve")
        s_tr_in = sem("s_tr_in")
        s_tr = sem("s_tr")
        s_carry_in = sem("s_carry_in")
        s_carry = sem("s_carry")
        s_exp_in = sem("s_exp_in")
        s_exp = sem("s_exp")
        s_pre_load = sem("s_pre_load")
        s_wexp = sem("s_wexp")
        s_sig = sem("s_sig")
        s_wstore = sem("s_wstore")
        s_wload = sem("s_wload")
        s_same_in = sem("s_same_in")
        s_same_out = sem("s_same_out")
        s_beta = sem("s_beta")
        s_cols_free = sem("s_cols_free")
        s_cols = sem("s_cols")
        s_deg = sem("s_deg")
        s_dinv = sem("s_dinv")
        edge_w = nc.dram_tensor("edge_w", (P, ET), FP32).ap()
        with ExitStack() as ph:
            dcur = sb("dcur", [P, C], I32, stack=ph)
            dprev = sb("dprev", [P, C], I32, stack=ph)
            dnext = sb("dnext", [P, C], I32, stack=ph)
            same_p = sb("same_p", [P, C], stack=ph)
            same_n = sb("same_n", [P, C], stack=ph)
            pen_p = sb("pen_p", [P, C], stack=ph)
            pen_n = sb("pen_n", [P, C], stack=ph)
            s_self = sb("s_self", [P, C], stack=ph)
            s_edge = sb("s_edge", [P, C], stack=ph)
            work = sb("work", [P, C], stack=ph)
            run1 = sb("run1", [P, C], stack=ph)
            run2 = sb("run2", [P, C], stack=ph)
            wpre = sb("wpre", [P, ET], stack=ph)
            same_bf = sb("same_bf", [K, C], BF16, stack=ph)
            open_f = sb("open_f", [P, 4], stack=ph)
            rows = sb("rows", [1, 2 * P], stack=ph)
            chain = sb("chain", [1, P + 2], stack=ph)
            carry = sb("carry", [P, 1], stack=ph)
            inv_d = sb("inv_d", [P, ET], stack=ph)
            ends = sb("ends", [P, 2], stack=ph)
            GRP = [(j, min(4, CT - j)) for j in range(0, CT, 4)]

            with nc.Block() as block:
                @block.sync
                def _(sp):
                    for r in range(H + 1):
                        for to, at in ((dcur, 1), (dprev, 0), (dnext, 2)):
                            sp.dma_start(to[r * K:(r + 1) * K, :], dst_ext[at:at + EP].rearrange("(k c) -> k c", k=K)
                                         ).then_inc(s_seg_load, 16)
                    sp.dma_start(wpre[:, :], edge_pre.rearrange("o (p c) -> (o p) c", p=P)).then_inc(s_pre_load, 16)
                    hold(sp, s_zeroed, 2, sp_gate)
                    sp.dma_start(s_self[0:SP_ROWS, :], scores[0:H, :].rearrange("h (k c) -> (h k) c", k=K)).then_inc(s_score_load, 16)
                    sp.dma_start(s_edge[0:SP_ROWS, :], scores[H:2 * H, :].rearrange("h (k c) -> (h k) c", k=K)).then_inc(s_score_load, 16)
                    hold(sp, s_sig, 1, sp_gate)
                    sp.dma_start(edge_w, wpre[:, :]).then_inc(s_wstore, 16)
                    hold(sp, s_same_in, 1, sp_gate)
                    sp.dma_start(same_row, same_bf[:, :]).then_inc(s_same_out, 16)
                    hold(sp, s_wstore, 16, sp_gate)
                    hold(sp, s_exp, 2, sp_gate)
                    sp.dma_start(s_edge[SP_ROWS:RP, :], edge_w.rearrange("p c -> (p c)").rearrange("(k c) -> k c", k=K)
                                 ).then_inc(s_wload, 16)
                    hold(sp, s_same_out, 16, sp_gate)

                @block.gpsimd
                def _(pool):
                    nc.gpsimd.memset(s_self[:, :], 0.0).then_inc(s_zeroed, 1)
                    nc.gpsimd.memset(s_edge[:, :], 0.0).then_inc(s_zeroed, 1)

                @block.scalar
                def _(act):
                    act.wait_ge(s_pre_load, 16)
                    nc.scalar.activation(wpre[:, :], wpre[:, :], ACT.Exp, scale=-1.0).then_inc(s_wexp, 1)
                    act.wait_ge(s_exp_in, 1)
                    nc.scalar.activation(s_edge[0:RP, :], run1[0:RP, :], ACT.Exp).then_inc(s_exp, 1)
                    act.wait_ge(s_exp_in, 2)
                    nc.scalar.activation(s_self[0:RP, :], work[0:RP, :], ACT.Exp).then_inc(s_exp, 1)
                    act.wait_ge(s_deg, 1)
                    nc.scalar.activation(dinv[:, :], deg_inv[:, :], ACT.Sqrt).then_inc(s_dinv, 1)

                @block.vector
                def _(dve):
                    done = [0]
                    scans = [0]

                    def link(ins):
                        done[0] += 1
                        ins.then_inc(s_dve, 1)
                        dve.wait_ge(s_dve, done[0])

                    def run_scan(to, keep, data, flag, op, back):
                        v = (lambda t: t[0:RP, ::-1]) if back else (lambda t: t[0:RP, :])
                        op1 = ALU.max if op == ALU.add else ALU.add
                        first = -HUGE if op == ALU.add else 0.0
                        link(nc.vector.tensor_tensor_scan(v(to), v(keep), v(data), first, op, op1))
                        link(nc.vector.tensor_copy(carry[0:RP, :], to[0:RP, 0:1] if back else to[0:RP, C - 1:C]))
                        scans[0] += 1
                        nc.vector.tensor_copy(ends[0:RP, 0:1], carry[0:RP, :])
                        nc.vector.tensor_copy(ends[0:RP, 1:2], open_f[0:RP, flag:flag + 1]).then_inc(s_tr_in, 1)
                        dve.wait_ge(s_tr, 2 * scans[0])
                        link(nc.vector.tensor_copy(rows[:, :], bank[0][0:1, 0:2 * P]))
                        link(nc.vector.memset(chain[:, :], 0.0))
                        w = slice(RP - 1, None, -1) if back else slice(0, RP)
                        o = slice(RP, 0, -1) if back else slice(1, RP + 1)
                        wf = slice(P + RP - 1, P - 1, -1) if back else slice(P, P + RP)
                        nc.vector.tensor_tensor_scan(chain[:, o], rows[:, wf], rows[:, w], first, op, op1).then_inc(s_carry_in, 1)
                        dve.wait_ge(s_carry, scans[0])
                        link(nc.vector.tensor_copy(carry[0:RP, :], bank[1][0:RP, 0:1]))
                        link(nc.vector.tensor_tensor_scan(v(to), v(keep), v(data), carry[0:RP, 0:1], op, op1))

                    dve.wait_ge(s_seg_load, 16 * 3 * (H + 1))
                    link(nc.vector.memset(ends[:, :], 0.0))
                    link(nc.vector.tensor_tensor(same_p[0:RP, :], dcur[0:RP, :], dprev[0:RP, :], ALU.is_equal))
                    link(nc.vector.tensor_tensor(same_n[0:RP, :], dcur[0:RP, :], dnext[0:RP, :], ALU.is_equal))
                    nc.vector.tensor_copy(same_bf[:, :], same_p[0:K, :]).then_inc(s_same_in, 1)
                    link(nc.vector.tensor_scalar(pen_p[0:RP, :], same_p[0:RP, :], -1.0, HUGE, ALU.add, ALU.mult))
                    link(nc.vector.tensor_scalar(pen_n[0:RP, :], same_n[0:RP, :], -1.0, HUGE, ALU.add, ALU.mult))
                    link(nc.vector.tensor_reduce(open_f[0:RP, 0:1], same_p[0:RP, :], AX.X, ALU.min))
                    link(nc.vector.tensor_reduce(open_f[0:RP, 1:2], same_n[0:RP, :], AX.X, ALU.min))
                    link(nc.vector.tensor_scalar(open_f[0:RP, 2:4], open_f[0:RP, 0:2], -1.0, HUGE, ALU.add, ALU.mult))
                    dve.wait_ge(s_wexp, 1)
                    link(nc.vector.tensor_scalar(wpre[:, :], wpre[:, :], 1.0, None, ALU.add))
                    nc.vector.reciprocal(wpre[:, :], wpre[:, :]).then_inc(s_sig, 1)
                    dve.wait_ge(s_score_load, 32)
                    link(nc.vector.tensor_tensor(work[0:RP, :], s_self[0:RP, :], s_edge[0:RP, :], ALU.max))
                    run_scan(run1, pen_p, work, 2, ALU.add, False)
                    run_scan(run2, pen_n, run1, 3, ALU.add, True)
                    nc.vector.tensor_tensor(run1[0:RP, :], s_edge[0:RP, :], run2[0:RP, :], ALU.subtract).then_inc(s_exp_in, 1)
                    nc.vector.tensor_tensor(work[0:RP, :], s_self[0:RP, :], run2[0:RP, :], ALU.subtract).then_inc(s_exp_in, 1)
                    dve.wait_ge(s_exp, 2)
                    dve.wait_ge(s_wload, 16)
                    run_scan(run1, same_p, s_edge, 0, ALU.mult, False)
                    link(nc.vector.tensor_tensor(work[0:RP, :], run1[0:RP, :], same_n[0:RP, :], ALU.mult))
                    link(nc.vector.tensor_tensor(work[0:RP, :], run1[0:RP, :], work[0:RP, :], ALU.subtract))
                    run_scan(run1, same_n, work, 1, ALU.mult, True)
                    link(nc.vector.tensor_tensor(work[0:RP, :], run1[0:RP, :], s_self[0:RP, :], ALU.add))
                    link(nc.vector.reciprocal(run2[0:RP, :], work[0:RP, :]))
                    nc.vector.scalar_tensor_tensor(run1[0:RP, :], s_edge[0:RP, :], gate_rows[0:RP, 0:1], run2[0:RP, :],
                                                   ALU.mult, ALU.mult).then_inc(s_beta, 1)
                    for n, (j, m) in enumerate(GRP):
                        dve.wait_ge(s_cols, n + 1)
                        src = bank[2 + n % 2][:, :].rearrange("p (j r) -> p j r", r=P)
                        to = beta_cols_sb[:, :, :].rearrange("p h (k j) -> p j (h k)", j=CT)
                        nc.vector.tensor_copy(to[:, j:j + m, :], src[:, 0:m, 0:RP])
                        src = bank[4 + n % 2][:, :].rearrange("p (j r) -> p j r", r=P)
                        to = deg_inv[:, :].rearrange("p (k j) -> p j k", j=CT)
                        last = nc.vector.tensor_copy(to[:, j:j + m, :], src[:, 0:m, SP_ROWS:RP])
                        last.then_inc(s_cols_free, 1)
                    dve.wait_ge(s_cols_free, len(GRP))
                    nc.vector.tensor_copy(inv_d[:, :], deg_inv[:, :]).then_inc(s_deg, 1)
                    dve.wait_ge(s_dinv, 1)
                    link(nc.vector.reciprocal(inv_d[:, :], dinv[:, :]))
                    link(nc.vector.tensor_tensor(beta_cols_sb[:, H, :], beta_cols_sb[:, H, :], inv_d[:, :], ALU.mult))

                @block.tensor
                def _(pe):
                    for n, back in enumerate((False, True, False, True)):
                        pe.wait_ge(s_tr_in, n + 1)
                        nc.tensor.transpose(bank[0][0:1, 0:RP], ends[0:RP, 0:1], ident[0:RP, 0:RP]).then_inc(s_tr, 1)
                        nc.tensor.transpose(bank[0][0:1, P:P + RP], ends[0:RP, 1:2], ident[0:RP, 0:RP]).then_inc(s_tr, 1)
                        pe.wait_ge(s_carry_in, n + 1)
                        at = 2 if back else 0
                        nc.tensor.matmul(bank[1][0:RP, 0:1], chain[0:1, at:at + RP], one[0:1, 0:1], start=True, stop=True
                                         ).then_inc(s_carry, 1)
                    pe.wait_ge(s_beta, 1)
                    for n, (j, m) in enumerate(GRP):
                        wait_reuse(pe, s_cols_free, n - 1)
                        for i in range(m):
                            e = (j + i) * P
                            nc.tensor.transpose(bank[2 + n % 2][:, i * P:i * P + RP], run1[0:RP, e:e + P], ident[0:RP, 0:RP])
                            last = nc.tensor.transpose(bank[4 + n % 2][:, i * P:i * P + RP], run2[0:RP, e:e + P],
                                                       ident[0:RP, 0:RP])
                        last.then_inc(s_cols, 1)

        mask = sb("mask", [P, EP], BF16)
        s_mask = sem("s_mask")

        b_load = [sem(f"b_load{s}") for s in range(2)]
        b_hi = sem("b_hi")
        b_lo = sem("b_lo")
        b_u = sem("b_u")
        b_init = sem("b_init")
        b_acc = sem("b_acc")
        b_sum = sem("b_sum")
        b_gt = sem("b_gt")
        b_scan = sem("b_scan")
        b_back = sem("b_back")
        b_evac = sem("b_evac")
        b_rowsum = sem("b_rowsum")
        b_pad = sem("b_pad")
        b_out = [sem(f"b_out{s}") for s in range(2)]
        b_idx = sem("b_idx")
        b_noted = [sem(f"b_noted{s}") for s in range(2)]
        NQ = H // 2
        with ExitStack() as ph:
            dt = sb("dt", [P, 2, A, BLK], stack=ph)
            hi = sb("hi", [P, 2, A, BLK], FP32R, stack=ph)
            lo = sb("lo", [P, 2, A, BLK], FP32R, stack=ph)
            acc = sb("acc", [P, 2, 2, D], stack=ph)
            gsum = sb("gsum_b", [P, 2, TB, D], stack=ph)
            pfx = sb("pfx", [P, 2, A, BLK], stack=ph)
            grow = sb("grow", [P, 2, TB, ROW], stack=ph)
            note = sb("note", [P, 2, 2 * TB], I32, stack=ph)

            with nc.Block() as block:
                @block.sync
                def _(sp):
                    def load(b, s, q):
                        hold(sp, b_lo, b - 1, sp_gate)
                        sp.dma_start(dt[:, s, :, :].rearrange("p a e -> p (a e)"),
                                     diff_t[bass.ds(b, 1), :, :].rearrange("o p c -> (o p) c")).then_inc(b_load[s], 16)

                    def store(b, s, q):
                        hold(sp, b_rowsum, b + 1, sp_gate)
                        sp.dma_start(gat_tab[bass.ds(b * BLK, BLK), :].rearrange("(t p) c -> p t c", p=P),
                                     grow[:, s, :, :]).then_inc(b_out[s], 16)
                    sp.dma_start(mask[:, :], same_row.rearrange("k c -> (k c)").partition_broadcast(P)).then_inc(s_mask, 16)
                    pipeline(sp, EB, 2, 2, [(0, load), (4, store)])
                    hold(sp, b_out[0], 16 * ((EB + 1) // 2), sp_gate)
                    hold(sp, b_out[1], 16 * (EB // 2), sp_gate)
                    hold(sp, s_mask, 16, sp_gate)

                @block.gpsimd
                def _(pool):
                    nc.gpsimd.memset(grow[:, :, :, :], 0.0).then_inc(b_pad, 1)
                    nc.gpsimd.memset(pfx[:, :, :, :], 0.0).then_inc(b_pad, 1)

                    def split(b, s, q):
                        hold(pool, b_hi, b + 1, pool_gate)
                        hold(pool, b_u, TB * NQ * (b - 1), pool_gate)
                        nc.gpsimd.tensor_tensor(lo[:, s, :, :], dt[:, s, :, :], hi[:, s, :, :].bitcast(FP32), ALU.subtract
                                                ).then_inc(b_lo, 1)

                    def note_last(b, s, q):
                        hold(pool, b_noted[s], 16 * TB * q, pool_gate)
                        nc.gpsimd.tensor_copy(note[:, s, 0:TB], scatter_to[:, bass.ds(b * TB, TB)]).then_inc(b_idx, 1)
                        nc.gpsimd.tensor_copy(note[:, s, TB:2 * TB], edge_ids[:, bass.ds(b * TB, TB)]).then_inc(b_idx, 1)
                        hold(pool, b_idx, 2 * (b + 1), pool_gate)
                        for t in range(TB):
                            nc.gpsimd.indirect_dma_start(
                                out=last_of[:, :], out_offset=bass.IndirectOffsetOnAxis(ap=note[:, s, t:t + 1], axis=0),
                                in_=note[:, s, TB + t:TB + t + 1], in_offset=None,
                                bounds_check=N - 1, oob_is_err=False).then_inc(b_noted[s], 16)

                    def finish(b, s, q):
                        hold(pool, b_evac, b + 1, pool_gate)
                        nc.gpsimd.tensor_tensor(grow[:, s, :, 0:D], grow[:, s, :, 0:D],
                                                bgat[:, :].unsqueeze(1).to_broadcast([P, TB, D]), ALU.add)
                        nc.gpsimd.tensor_copy(grow[:, s, :, D:D + 1],
                                              dinv[:, bass.ds(b * TB, TB)].unsqueeze(2)).then_inc(b_rowsum, 1)
                    pipeline(pool, EB, 2, 2, [(0, split), (1, note_last), (4, finish)])
                    hold(pool, b_noted[0], 16 * TB * ((EB + 1) // 2), pool_gate)
                    hold(pool, b_noted[1], 16 * TB * (EB // 2), pool_gate)

                @block.scalar
                def _(act):
                    def split(b, s, q):
                        act.wait_ge(b_load[s], 16 * (q + 1))
                        wait_reuse(act, b_u, TB * NQ * (b - 1))
                        nc.scalar.activation(hi[:, s, :, :], dt[:, s, :, :], ACT.Copy).then_inc(b_hi, 1)

                    def init(b, s, q):
                        for t in range(TB):
                            act.wait_ge(b_u, TB * NQ * b + NQ * t + 1)
                            wait_reuse(act, b_sum, TB * b + t - 1)
                            for h in range(2):
                                last = nc.scalar.activation(acc[:, t % 2, h, :], bank[0][:, h * D:(h + 1) * D], ACT.Copy,
                                                            scale=beta_cols_sb[:, h, bass.ds(b * TB + t, 1)])
                            last.then_inc(b_init, 1)

                    def evacuate(b, s, q):
                        act.wait_ge(b_back, b + 1)
                        wait_reuse(act, b_out[s], 16 * q)
                        act.wait_ge(b_pad, 2)
                        for half in range(2):
                            last = nc.scalar.activation(grow[:, s, 2 * half:2 * half + 2, 0:D],
                                                        bank[6 + half][:, :].rearrange("p (t d) -> p t d", d=D), ACT.Copy)
                        last.then_inc(b_evac, 1)
                    pipeline(act, EB, 2, 2, [(0, split), (1, init), (3, evacuate)])

                @block.vector
                def _(dve):
                    def accumulate(b, s, q):
                        for t in range(TB):
                            u = TB * b + t
                            for n in range(1, NQ):
                                dve.wait_ge(b_u, NQ * u + n + 1)
                                if n == 1:
                                    dve.wait_ge(b_init, u + 1)
                                    wait_reuse(dve, b_gt, b - 1)
                                for h in range(2):
                                    if n > 1:
                                        dve.wait_ge(b_acc, 6 * u + 2 * n - 3 + h)
                                    nc.vector.scalar_tensor_tensor(
                                        acc[:, t % 2, h, :], bank[n][:, h * D:(h + 1) * D],
                                        beta_cols_sb[:, 2 * n + h, bass.ds(u, 1)], acc[:, t % 2, h, :],
                                        ALU.mult, ALU.add).then_inc(b_acc, 1)
                            dve.wait_ge(b_acc, 6 * u + 6)
                            nc.vector.tensor_tensor(gsum[:, s, t, :], acc[:, t % 2, 0, :], acc[:, t % 2, 1, :], ALU.add
                                                    ).then_inc(b_sum, 1)

                    def scan(b, s, q):
                        dve.wait_ge(b_gt, b + 1)
                        wait_reuse(dve, b_back, b - 1)
                        wait_reuse(dve, b_scan, b)
                        for a in range(A):
                            last = nc.vector.tensor_tensor_scan(
                                pfx[:, s, a, :], mask[:, bass.ds(b * BLK, BLK)], bank[4 + a][:, :],
                                pfx[:, 1 - s, a, BLK - 1:BLK], ALU.mult, ALU.add)
                        last.then_inc(b_scan, 1)
                    dve.wait_ge(b_pad, 2)
                    dve.wait_ge(s_mask, 16)
                    pipeline(dve, EB, 2, 2, [(1, accumulate), (2, scan)])

                @block.tensor
                def _(pe):
                    def products(b, s, q):
                        pe.wait_ge(b_hi, b + 1)
                        pe.wait_ge(b_lo, b + 1)
                        for t in range(TB):
                            u = TB * b + t
                            e = slice(t * P, (t + 1) * P)
                            for n in range(NQ):
                                w = slice(2 * n * D, 2 * (n + 1) * D)
                                if n == 0:
                                    wait_reuse(pe, b_init, u)
                                else:
                                    wait_reuse(pe, b_acc, 6 * (u - 1) + 2 * n)
                                for a in range(A):
                                    nc.tensor.matmul(bank[n][:, :], hi[:, s, a, e], w_hi[:, a, w], start=a == 0, stop=False)
                                    nc.tensor.matmul(bank[n][:, :], hi[:, s, a, e], w_lo[:, a, w], start=False, stop=False)
                                    last = nc.tensor.matmul(bank[n][:, :], lo[:, s, a, e], w_hi[:, a, w], start=False,
                                                            stop=a == A - 1)
                                last.then_inc(b_u, 1)

                    def transpose(b, s, q):
                        pe.wait_ge(b_sum, TB * (b + 1))
                        wait_reuse(pe, b_scan, b)
                        for t in range(TB):
                            for a in range(A):
                                last = nc.tensor.transpose(bank[4 + a][:, t * P:(t + 1) * P],
                                                           gsum[:, s, t, a * P:(a + 1) * P], ident[:, :])
                        last.then_inc(b_gt, 1)

                    def back(b, s, q):
                        pe.wait_ge(b_scan, b + 1)
                        wait_reuse(pe, b_evac, b)
                        for t in range(TB):
                            for a in range(A):
                                at = (t % 2) * D + a * P
                                last = nc.tensor.transpose(bank[6 + t // 2][:, at:at + P],
                                                           pfx[:, s, a, t * P:(t + 1) * P], ident[:, :])
                        last.then_inc(b_back, 1)
                    pipeline(pe, EB, 2, 2, [(1, products), (2, transpose), (3, back)])

        c_x = [sem(f"c_x{s}") for s in range(2)]
        c_last = [sem(f"c_last{s}") for s in range(2)]
        c_fill = sem("c_fill")
        c_tmpl = sem("c_tmpl")
        c_rows = [sem(f"c_rows{s}") for s in range(2)]
        c_xb = sem("c_xb")
        c_dinv = sem("c_dinv")
        c_xt = sem("c_xt")
        c_xt_sb = sem("c_xt_sb")
        c_res = sem("c_res")
        c_res_sb = sem("c_res_sb")
        c_mv = sem("c_mv")
        c_agg = sem("c_agg")
        c_rt = sem("c_rt")
        c_rt_sb = sem("c_rt_sb")
        c_o = sem("c_o")
        c_std = sem("c_std")
        c_rstd = sem("c_rstd")
        c_y = sem("c_y")
        c_mv2 = sem("c_mv2")
        c_agg2 = sem("c_agg2")
        c_std2 = sem("c_std2")
        c_rstd2 = sem("c_rstd2")
        c_shift = sem("c_shift")
        c_fin = sem("c_fin")
        c_out = [sem(f"c_out{s}") for s in range(2)]
        U = 2 * TB
        OUT_LAG = 6
        FIN_LAG = 12

        def node_rows(table, b, width, last):
            base = LAST_BASE if last else b * BLK
            return table[bass.ds(base, BLK), 0:width].rearrange("(p t) c -> p t c", p=P)

        def blocks(eng, depth, steps):
            most = max(lag for lag, _ in steps)
            head = 2 * (-(-(most + depth) // 2))

            def peeled(turn):
                for lag, fn in steps:
                    g = turn - lag
                    if 0 <= g < NB:
                        fn(g, g % 2, g // 2, g == NB - 1)

            for turn in range(head):
                peeled(turn)
            with eng.Fori(head // 2, NB // 2 - 1) as j:
                for r in range(2):
                    for lag, fn in steps:
                        fn(j * 2 + (r - lag), (r - lag) % 2, j + (r - lag) // 2, False)
            for turn in range(NB - 2, NB + most):
                peeled(turn)

        with ExitStack() as ph:
            xin = sb("xin", [P, 2, TB, D], stack=ph)
            xb = sb("xb", [P, 2, TB, D], stack=ph)
            lidx = sb("lidx", [P, 2, TB], I32, stack=ph)
            fill = sb("fill", [P, TB, ROW], stack=ph)
            gin = sb("gin", [P, 2, TB, ROW], stack=ph)
            xt = sb("xt", [P, 2, A, P], stack=ph)
            res = sb("res", [P, 2, D], stack=ph)
            rt = sb("rt", [P, U, A, P], stack=ph)
            y = sb("y", [P, 2, TB, D], stack=ph)
            xo = sb("xo", [P, 2, TB, ROW], stack=ph)
            st = sb("st", [P, 2, 6], stack=ph)
            mv = sb("mv", [P, 2, TB, 2], stack=ph)
            st2 = sb("st2", [P, 2, 6], stack=ph)
            mv2 = sb("mv2", [P, 2, TB, 2], stack=ph)
            rstd = sb("rstd", [P, 2, TB], stack=ph)
            rstd2 = sb("rstd2", [P, 2, TB], stack=ph)
            shift = sb("shift", [P, 2, TB], stack=ph)

            with nc.Block() as block:
                @block.sync
                def _(sp):
                    def load(b, s, q, last):
                        hold(sp, c_xb, b - 1, sp_gate)
                        hold(sp, c_xt, TB * (b - 1), sp_gate)
                        sp.dma_start(xin[:, s, :, :], node_rows(x, b, D, last)).then_inc(c_x[s], 16)
                        hold(sp, c_rows[s], 16 * TB * q, sp_gate)
                        sp.dma_start(lidx[:, s, :], last_of[bass.ds(LAST_BASE if last else b * BLK, BLK), :]
                                     .rearrange("(p t) o -> p (t o)", p=P)).then_inc(c_last[s], 16)

                    def store(b, s, q, last):
                        hold(sp, c_fin, TB * (b + 1), sp_gate)
                        hold(sp, c_dinv, b + 1, sp_gate)
                        if last:
                            hold(sp, c_out[1 - s], 16 * (q + 1), sp_gate)
                        sp.dma_start(node_rows(x1_tab, b, ROW, last), xo[:, s, :, :]).then_inc(c_out[s], 16)
                    blocks(sp, 2, [(0, load), (4, store)])
                    hold(sp, c_out[0], 16 * (NB // 2), sp_gate)
                    hold(sp, c_out[1], 16 * (NB // 2), sp_gate)

                @block.gpsimd
                def _(pool):
                    nc.gpsimd.memset(xo[:, :, :, :], 0.0).then_inc(c_tmpl, 1)
                    nc.gpsimd.memset(fill[:, :, :], 0.0).then_inc(c_tmpl, 1)
                    hold(pool, c_tmpl, 2, pool_gate)
                    nc.gpsimd.memset(fill[:, :, D:D + 1], 1.0).then_inc(c_tmpl, 1)
                    nc.gpsimd.tensor_copy(fill[:, :, 0:D], bgat[:, :].unsqueeze(1).to_broadcast([P, TB, D])).then_inc(c_tmpl, 1)
                    hold(pool, c_tmpl, 4, pool_gate)

                    def gather(b, s, q, last):
                        hold(pool, c_res_sb, TB * (b - 1), pool_gate)
                        hold(pool, c_dinv, b - 1, pool_gate)
                        nc.gpsimd.tensor_copy(gin[:, s, :, :], fill[:, :, :]).then_inc(c_fill, 1)
                        hold(pool, c_fill, b + 1, pool_gate)
                        hold(pool, c_last[s], 16 * (q + 1), pool_gate)
                        for t in range(TB):
                            nc.gpsimd.indirect_dma_start(
                                out=gin[:, s, t, :], out_offset=None, in_=gat_tab[:, :],
                                in_offset=bass.IndirectOffsetOnAxis(ap=lidx[:, s, t:t + 1], axis=0),
                                bounds_check=EP - 1, oob_is_err=False).then_inc(c_rows[s], 16)

                    def residual(b, s, q, last):
                        hold(pool, c_x[s], 16 * (q + 1), pool_gate)
                        hold(pool, c_y, TB * (b - 1), pool_gate)
                        nc.gpsimd.tensor_tensor(xb[:, s, :, :], xin[:, s, :, :],
                                                out_bias[:, :].unsqueeze(1).to_broadcast([P, TB, D]), ALU.add).then_inc(c_xb, 1)
                        hold(pool, c_rows[s], 16 * TB * (q + 1), pool_gate)
                        hold(pool, c_out[s], 16 * q, pool_gate)
                        nc.gpsimd.tensor_copy(xo[:, s, :, D:D + 1], gin[:, s, :, D:D + 1]).then_inc(c_dinv, 1)
                    blocks(pool, 2, [(0, gather), (1, residual)])

                @block.tensor
                def _(pe):
                    def x_transpose(g, r, q):
                        if r % TB == 0:
                            pe.wait_ge(c_x[r // TB], 16 * (q + 1))
                        wait_reuse(pe, c_xt_sb, g - 1)
                        for a in range(A):
                            last = nc.tensor.transpose(bank[r % 2][:, a * P:(a + 1) * P],
                                                       xin[:, r // TB, r % TB, a * P:(a + 1) * P], ident[:, :])
                        last.then_inc(c_xt, 1)

                    def residual(g, r, q):
                        pe.wait_ge(c_xt_sb, g + 1)
                        wait_reuse(pe, c_res_sb, g - 1)
                        for a in range(A):
                            last = nc.tensor.matmul(bank[2 + r % 2][:, 0:D], xt[:, r % 2, a, :], m1[:, a, :],
                                                    start=a == 0, stop=a == A - 1)
                        last.then_inc(c_res, 1)

                    def res_transpose(g, r, q):
                        pe.wait_ge(c_res_sb, g + 1)
                        wait_reuse(pe, c_rt_sb, g - 1)
                        for a in range(A):
                            last = nc.tensor.transpose(bank[4 + r % 2][:, a * P:(a + 1) * P],
                                                       res[:, r % 2, a * P:(a + 1) * P], ident[:, :])
                        last.then_inc(c_rt, 1)

                    def project(g, r, q):
                        pe.wait_ge(c_rt_sb, g + 1)
                        wait_reuse(pe, c_y, g - 1)
                        for a in range(A):
                            last = nc.tensor.matmul(bank[6 + r % 2][:, 0:D], rt[:, r, a, :], cwo[:, a, :],
                                                    start=a == 0, stop=a == A - 1)
                        last.then_inc(c_o, 1)
                    pipeline(pe, NT, U, 2, [(0, x_transpose), (1, residual), (2, res_transpose), (OUT_LAG, project)])

                @block.scalar
                def _(act):
                    def x_evacuate(g, r, q):
                        act.wait_ge(c_xt, g + 1)
                        wait_reuse(act, c_res, g - 1)
                        nc.scalar.activation(xt[:, r % 2, :, :], bank[r % 2][:, 0:D].rearrange("p (a e) -> p a e", a=A), ACT.Copy
                                             ).then_inc(c_xt_sb, 1)

                    def res_evacuate(g, r, q):
                        act.wait_ge(c_rt, g + 1)
                        wait_reuse(act, c_o, g + 1 - U)
                        nc.scalar.activation(rt[:, r, :, :], bank[4 + r % 2][:, 0:D].rearrange("p (a e) -> p a e", a=A), ACT.Copy
                                             ).then_inc(c_rt_sb, 1)

                    def std(g, r, q):
                        if r % TB == TB - 1:
                            s = r // TB
                            act.wait_ge(c_agg, g + 1)
                            nc.scalar.activation(rstd[:, s, :], mv[:, s, :, 1], ACT.Sqrt, bias=eps_col[:, 0:1]).then_inc(c_std, 1)

                    def std2(g, r, q):
                        if r % TB == TB - 1:
                            s = r // TB
                            act.wait_ge(c_agg2, g + 1)
                            nc.scalar.activation(rstd2[:, s, :], mv2[:, s, :, 1], ACT.Sqrt, bias=eps_col[:, 0:1]).then_inc(c_std2, 1)

                    def finish(g, r, q):
                        s, t = r // TB, r % TB
                        if t == 0:
                            act.wait_ge(c_shift, 2 * q + s + 1)
                            wait_reuse(act, c_out[s], 16 * q)
                            act.wait_ge(c_tmpl, 1)
                        nc.scalar.activation(xo[:, s, t, 0:D], y[:, s, t, :], ACT.Identity, bias=shift[:, s, t:t + 1],
                                             scale=rstd2[:, s, t:t + 1]).then_inc(c_fin, 1)
                    pipeline(act, NT, U, U, [(0, x_evacuate), (2, res_evacuate), (1, std), (OUT_LAG, std2), (FIN_LAG, finish)])

                @block.vector
                def _(dve):
                    def add_rows(g, r, q):
                        s, t = r // TB, r % TB
                        dve.wait_ge(c_res, g + 1)
                        if t == 0:
                            dve.wait_ge(c_rows[s], 16 * TB * (q + 1))
                        wait_reuse(dve, c_rt, g - 1)
                        nc.vector.tensor_tensor(res[:, r % 2, :], gin[:, s, t, 0:D], bank[2 + r % 2][:, 0:D], ALU.add
                                                ).then_inc(c_res_sb, 1)

                    def stats(g, r, q):
                        dve.wait_ge(c_res_sb, g + 1)
                        nc.vector.bn_stats(st[:, r % 2, :], res[:, r % 2, :]).then_inc(c_mv, 1)

                    def aggregate(g, r, q):
                        hold(dve, c_mv, g + 1, dve_gate)
                        if r % TB == 0:
                            hold(dve, c_std, 2 * q + r // TB - 1, dve_gate)
                        nc.vector.bn_aggr(mv[:, r // TB, r % TB, :], st[:, r % 2, :]).then_inc(c_agg, 1)

                    def scale(g, r, q):
                        if r % TB == TB - 1:
                            s = r // TB
                            dve.wait_ge(c_std, 2 * q + s + 1)
                            nc.vector.reciprocal(rstd[:, s, :], rstd[:, s, :]).then_inc(c_rstd, 1)

                    def add_residual(g, r, q):
                        s, t = r // TB, r % TB
                        dve.wait_ge(c_o, g + 1)
                        if t == 0:
                            dve.wait_ge(c_rstd, 2 * q + s + 1)
                            dve.wait_ge(c_xb, 2 * q + s + 1)
                            wait_reuse(dve, c_fin, g + TB - U)
                        nc.vector.scalar_tensor_tensor(y[:, s, t, :], bank[6 + r % 2][:, 0:D], rstd[:, s, t:t + 1],
                                                       xb[:, s, t, :], ALU.mult, ALU.add).then_inc(c_y, 1)

                    def stats2(g, r, q):
                        dve.wait_ge(c_y, g + 1)
                        nc.vector.bn_stats(st2[:, r % 2, :], y[:, r // TB, r % TB, :]).then_inc(c_mv2, 1)

                    def aggregate2(g, r, q):
                        hold(dve, c_mv2, g + 1, dve_gate)
                        if r % TB == 0:
                            hold(dve, c_shift, 2 * q + r // TB - 1, dve_gate)
                        nc.vector.bn_aggr(mv2[:, r // TB, r % TB, :], st2[:, r % 2, :]).then_inc(c_agg2, 1)

                    def scale2(g, r, q):
                        if r % TB == TB - 1:
                            s = r // TB
                            dve.wait_ge(c_std2, 2 * q + s + 1)
                            nc.vector.reciprocal(rstd2[:, s, :], rstd2[:, s, :]).then_inc(c_rstd2, 1)
                            dve.wait_ge(c_rstd2, 2 * q + s + 1)
                            nc.vector.scalar_tensor_tensor(shift[:, s, :], mv2[:, s, :, 0], -1.0, rstd2[:, s, :],
                                                           ALU.mult, ALU.mult).then_inc(c_shift, 1)
                    pipeline(dve, NT, U, U, [(0, add_rows), (OUT_LAG, add_residual), (0, stats), (OUT_LAG, stats2),
                                             (0, aggregate), (OUT_LAG, aggregate2), (1, scale), (OUT_LAG + 1, scale2)])

        d_idx = sem("d_idx")
        d_rows = [sem(f"d_rows{s}") for s in range(2)]
        d_coef = sem("d_coef")
        d_scaled = sem("d_scaled")
        d_t_ps = sem("d_t_ps")
        d_scan = sem("d_scan")
        d_back = sem("d_back")
        d_evac = sem("d_evac")
        d_fac = sem("d_fac")
        d_pad = sem("d_pad")
        d_out = [sem(f"d_out{s}") for s in range(2)]
        with ExitStack() as ph:
            idx = sb("idx_d", [P, 2, TB], I32, stack=ph)
            xr = sb("xr", [P, 2, TB, ROW], stack=ph)
            coef = sb("coef", [P, 2, TB], stack=ph)
            scaled = sb("scaled", [P, 2, TB, D], stack=ph)
            pfx = sb("pfx_d", [P, 2, A, BLK], stack=ph)
            trow = sb("trow", [P, 2, TB, ROW], stack=ph)

            with nc.Block() as block:
                @block.gpsimd
                def _(pool):
                    nc.gpsimd.memset(trow[:, :, :, :], 0.0).then_inc(d_pad, 1)
                    nc.gpsimd.memset(pfx[:, :, :, :], 0.0).then_inc(d_pad, 1)

                    def gather(b, s, q):
                        hold(pool, d_scaled, TB * (b - 1), pool_gate)
                        nc.gpsimd.tensor_copy(idx[:, s, :], idx_cols[:, bass.ds(b, 1), 0:TB].rearrange("p o c -> p (o c)")
                                              ).then_inc(d_idx, 1)
                        hold(pool, d_idx, b + 1, pool_gate)
                        for t in range(TB):
                            nc.gpsimd.indirect_dma_start(
                                out=xr[:, s, t, :], out_offset=None, in_=x1_tab[:, :],
                                in_offset=bass.IndirectOffsetOnAxis(ap=idx[:, s, t:t + 1], axis=0),
                                bounds_check=N - 1, oob_is_err=False).then_inc(d_rows[s], 16)
                    pipeline(pool, EB, 2, 2, [(0, gather)])

                @block.vector
                def _(dve):
                    def coefficient(b, s, q):
                        dve.wait_ge(d_rows[s], 16 * TB * (q + 1))
                        wait_reuse(dve, d_scaled, TB * (b - 1))
                        nc.vector.tensor_tensor(coef[:, s, :], beta_cols_sb[:, H, bass.ds(b * TB, TB)], xr[:, s, :, D], ALU.mult
                                                ).then_inc(d_coef, 1)

                    def scan(b, s, q):
                        dve.wait_ge(d_t_ps, b + 1)
                        wait_reuse(dve, d_back, b - 1)
                        wait_reuse(dve, d_scan, b)
                        for a in range(A):
                            last = nc.vector.tensor_tensor_scan(
                                pfx[:, s, a, :], mask[:, bass.ds(b * BLK, BLK)], bank[a][:, :],
                                pfx[:, 1 - s, a, BLK - 1:BLK], ALU.mult, ALU.add)
                        last.then_inc(d_scan, 1)

                    def factor(b, s, q):
                        wait_reuse(dve, d_out[s], 16 * q)
                        nc.vector.tensor_copy(trow[:, s, :, D:D + 1], deg_inv[:, bass.ds(b * TB, TB)].unsqueeze(2)
                                              ).then_inc(d_fac, 1)
                    dve.wait_ge(d_pad, 2)
                    pipeline(dve, EB, 2, 2, [(0, coefficient), (1, scan), (2, factor)])

                @block.scalar
                def _(act):
                    def scale(b, s, q):
                        act.wait_ge(d_coef, b + 1)
                        wait_reuse(act, d_t_ps, b - 1)
                        for t in range(TB):
                            nc.scalar.activation(scaled[:, s, t, :], xr[:, s, t, 0:D], ACT.Copy, scale=coef[:, s, t:t + 1]
                                                 ).then_inc(d_scaled, 1)

                    def evacuate(b, s, q):
                        act.wait_ge(d_back, b + 1)
                        wait_reuse(act, d_out[s], 16 * q)
                        act.wait_ge(d_pad, 1)
                        for half in range(2):
                            last = nc.scalar.activation(trow[:, s, 2 * half:2 * half + 2, 0:D],
                                                        bank[2 + half][:, :].rearrange("p (t d) -> p t d", d=D), ACT.Copy)
                        last.then_inc(d_evac, 1)
                    pipeline(act, EB, 2, 2, [(0, scale), (2, evacuate)])

                @block.tensor
                def _(pe):
                    def transpose(b, s, q):
                        pe.wait_ge(d_scaled, TB * (b + 1))
                        wait_reuse(pe, d_scan, b)
                        for t in range(TB):
                            for a in range(A):
                                last = nc.tensor.transpose(bank[a][:, t * P:(t + 1) * P],
                                                           scaled[:, s, t, a * P:(a + 1) * P], ident[:, :])
                        last.then_inc(d_t_ps, 1)

                    def back(b, s, q):
                        pe.wait_ge(d_scan, b + 1)
                        wait_reuse(pe, d_evac, b)
                        for t in range(TB):
                            for a in range(A):
                                at = (t % 2) * D + a * P
                                last = nc.tensor.transpose(bank[2 + t // 2][:, at:at + P],
                                                           pfx[:, s, a, t * P:(t + 1) * P], ident[:, :])
                        last.then_inc(d_back, 1)
                    pipeline(pe, EB, 2, 2, [(0, transpose), (1, back)])

                @block.sync
                def _(sp):
                    def store(b, s, q):
                        hold(sp, d_evac, b + 1, sp_gate)
                        hold(sp, d_fac, b + 1, sp_gate)
                        sp.dma_start(gcn_tab[bass.ds(b * BLK, BLK), :].rearrange("(t p) c -> p t c", p=P),
                                     trow[:, s, :, :]).then_inc(d_out[s], 16)
                    pipeline(sp, EB, 2, 2, [(0, store)])
                    hold(sp, d_out[0], 16 * ((EB + 1) // 2), sp_gate)
                    hold(sp, d_out[1], 16 * (EB // 2), sp_gate)

        e_x = [sem(f"e_x{s}") for s in range(2)]
        e_last = [sem(f"e_last{s}") for s in range(2)]
        e_fill = sem("e_fill")
        e_tmpl = sem("e_tmpl")
        e_rows = [sem(f"e_rows{s}") for s in range(2)]
        e_xb = sem("e_xb")
        e_mix = sem("e_mix")
        e_rt = sem("e_rt")
        e_rt_sb = sem("e_rt_sb")
        e_o = sem("e_o")
        e_y = sem("e_y")
        e_mv = sem("e_mv")
        e_agg = sem("e_agg")
        e_std = sem("e_std")
        e_rstd = sem("e_rstd")
        e_shift = sem("e_shift")
        e_fin = sem("e_fin")
        e_out = [sem(f"e_out{s}") for s in range(2)]
        with ExitStack() as ph:
            xin = sb("x1in", [P, 2, TB, D], stack=ph)
            xb = sb("x1b", [P, 2, TB, D], stack=ph)
            lidx = sb("lidx_e", [P, 2, TB], I32, stack=ph)
            fill = sb("fill_e", [P, TB, ROW], stack=ph)
            gin = sb("gin_e", [P, 2, TB, ROW], stack=ph)
            mix = sb("mix", [P, 2, D], stack=ph)
            rt = sb("rt_e", [P, 2, A, P], stack=ph)
            y = sb("y_e", [P, 2, TB, D], stack=ph)
            xo = sb("xo_e", [P, 2, TB, D], stack=ph)
            st = sb("st_e", [P, 2, 6], stack=ph)
            mv = sb("mv_e", [P, 2, TB, 2], stack=ph)
            rstd = sb("rstd_e", [P, 2, TB], stack=ph)
            shift = sb("shift_e", [P, 2, TB], stack=ph)

            with nc.Block() as block:
                @block.sync
                def _(sp):
                    def load(b, s, q, last):
                        hold(sp, e_xb, b - 1, sp_gate)
                        hold(sp, e_mix, TB * (b - 1), sp_gate)
                        sp.dma_start(xin[:, s, :, :], node_rows(x1_tab, b, D, last)).then_inc(e_x[s], 16)
                        hold(sp, e_rows[s], 16 * TB * q, sp_gate)
                        sp.dma_start(lidx[:, s, :], last_of[bass.ds(LAST_BASE if last else b * BLK, BLK), :]
                                     .rearrange("(p t) o -> p (t o)", p=P)).then_inc(e_last[s], 16)

                    def store(b, s, q, last):
                        hold(sp, e_fin, TB * (b + 1), sp_gate)
                        if last:
                            hold(sp, e_out[1 - s], 16 * (q + 1), sp_gate)
                        sp.dma_start(node_rows(out, b, D, last), xo[:, s, :, :]).then_inc(e_out[s], 16)
                    blocks(sp, 2, [(0, load), (3, store)])
                    hold(sp, e_out[0], 16 * (NB // 2), sp_gate)
                    hold(sp, e_out[1], 16 * (NB // 2), sp_gate)

                @block.gpsimd
                def _(pool):
                    nc.gpsimd.memset(fill[:, :, :], 0.0).then_inc(e_tmpl, 1)
                    hold(pool, e_tmpl, 1, pool_gate)
                    nc.gpsimd.memset(fill[:, :, D:D + 1], 1.0).then_inc(e_tmpl, 1)
                    hold(pool, e_tmpl, 2, pool_gate)

                    def gather(b, s, q, last):
                        hold(pool, e_mix, TB * (b - 1), pool_gate)
                        nc.gpsimd.tensor_copy(gin[:, s, :, :], fill[:, :, :]).then_inc(e_fill, 1)
                        hold(pool, e_fill, b + 1, pool_gate)
                        hold(pool, e_last[s], 16 * (q + 1), pool_gate)
                        for t in range(TB):
                            nc.gpsimd.indirect_dma_start(
                                out=gin[:, s, t, :], out_offset=None, in_=gcn_tab[:, :],
                                in_offset=bass.IndirectOffsetOnAxis(ap=lidx[:, s, t:t + 1], axis=0),
                                bounds_check=EP - 1, oob_is_err=False).then_inc(e_rows[s], 16)

                    def residual(b, s, q, last):
                        hold(pool, e_x[s], 16 * (q + 1), pool_gate)
                        hold(pool, e_y, TB * (b - 1), pool_gate)
                        nc.gpsimd.tensor_tensor(xb[:, s, :, :], xin[:, s, :, :],
                                                bc_row[:, :].unsqueeze(1).to_broadcast([P, TB, D]), ALU.add).then_inc(e_xb, 1)
                    blocks(pool, 2, [(0, gather), (1, residual)])

                @block.tensor
                def _(pe):
                    def transpose(g, r, q):
                        pe.wait_ge(e_mix, g + 1)
                        wait_reuse(pe, e_rt_sb, g - 1)
                        for a in range(A):
                            last = nc.tensor.transpose(bank[r % 2][:, a * P:(a + 1) * P], mix[:, r % 2, a * P:(a + 1) * P],
                                                       ident[:, :])
                        last.then_inc(e_rt, 1)

                    def project(g, r, q):
                        pe.wait_ge(e_rt_sb, g + 1)
                        wait_reuse(pe, e_y, g - 1)
                        for a in range(A):
                            last = nc.tensor.matmul(bank[2 + r % 2][:, 0:D], rt[:, r % 2, a, :], wc[:, a, :],
                                                    start=a == 0, stop=a == A - 1)
                        last.then_inc(e_o, 1)
                    pipeline(pe, NT, U, 2, [(0, transpose), (1, project)])

                @block.scalar
                def _(act):
                    def evacuate(g, r, q):
                        act.wait_ge(e_rt, g + 1)
                        wait_reuse(act, e_o, g - 1)
                        nc.scalar.activation(rt[:, r % 2, :, :], bank[r % 2][:, 0:D].rearrange("p (a e) -> p a e", a=A), ACT.Copy
                                             ).then_inc(e_rt_sb, 1)

                    def std(g, r, q):
                        if r % TB == TB - 1:
                            s = r // TB
                            act.wait_ge(e_agg, g + 1)
                            nc.scalar.activation(rstd[:, s, :], mv[:, s, :, 1], ACT.Sqrt, bias=eps_col[:, 0:1]).then_inc(e_std, 1)

                    def finish(g, r, q):
                        s, t = r // TB, r % TB
                        if t == 0:
                            act.wait_ge(e_shift, 2 * q + s + 1)
                            wait_reuse(act, e_out[s], 16 * q)
                        nc.scalar.activation(xo[:, s, t, :], y[:, s, t, :], ACT.Identity, bias=shift[:, s, t:t + 1],
                                             scale=rstd[:, s, t:t + 1]).then_inc(e_fin, 1)
                    pipeline(act, NT, U, U, [(0, evacuate), (2, std), (7, finish)])

                @block.vector
                def _(dve):
                    def mix_rows(g, r, q):
                        s, t = r // TB, r % TB
                        if t == 0:
                            dve.wait_ge(e_rows[s], 16 * TB * (q + 1))
                            dve.wait_ge(e_x[s], 16 * (q + 1))
                        wait_reuse(dve, e_rt, g - 1)
                        nc.vector.scalar_tensor_tensor(mix[:, r % 2, :], xin[:, s, t, :], gin[:, s, t, D:D + 1],
                                                       gin[:, s, t, 0:D], ALU.mult, ALU.add).then_inc(e_mix, 1)

                    def add_residual(g, r, q):
                        s, t = r // TB, r % TB
                        dve.wait_ge(e_o, g + 1)
                        if t == 0:
                            dve.wait_ge(e_xb, 2 * q + s + 1)
                            wait_reuse(dve, e_fin, g + TB - U)
                        nc.vector.tensor_tensor(y[:, s, t, :], xb[:, s, t, :], bank[2 + r % 2][:, 0:D], ALU.add).then_inc(e_y, 1)

                    def stats(g, r, q):
                        dve.wait_ge(e_y, g + 1)
                        nc.vector.bn_stats(st[:, r % 2, :], y[:, r // TB, r % TB, :]).then_inc(e_mv, 1)

                    def aggregate(g, r, q):
                        hold(dve, e_mv, g + 1, dve_gate)
                        if r % TB == 0:
                            hold(dve, e_shift, 2 * q + r // TB - 1, dve_gate)
                        nc.vector.bn_aggr(mv[:, r // TB, r % TB, :], st[:, r % 2, :]).then_inc(e_agg, 1)

                    def scale(g, r, q):
                        if r % TB == TB - 1:
                            s = r // TB
                            dve.wait_ge(e_std, 2 * q + s + 1)
                            nc.vector.reciprocal(rstd[:, s, :], rstd[:, s, :]).then_inc(e_rstd, 1)
                            dve.wait_ge(e_rstd, 2 * q + s + 1)
                            nc.vector.scalar_tensor_tensor(shift[:, s, :], mv[:, s, :, 0], -1.0, rstd[:, s, :],
                                                           ALU.mult, ALU.mult).then_inc(e_shift, 1)
                    pipeline(dve, NT, U, U, [(0, mix_rows), (2, add_residual), (2, stats), (2, aggregate), (3, scale)])


def kernel(x, src, dst, edge_attr_3, L0_gnn_W, L0_gnn_att_src, L0_gnn_att_dst, L0_gnn_bias_gat, L0_gnn_gate_weights,
           L0_gnn_ln_gamma, L0_gnn_ln_beta, L0_gnn_Wo, L0_gnn_bo, L1_gnn_W1, L1_gnn_b1, L1_gnn_W2, L1_gnn_b2,
           L1_gnn_Wc, L1_gnn_bc):
    import concourse.bacc as _bacc
    from concourse.bass_utils import run_bass_kernel_spmd as _run

    src, dst, attr = np.asarray(src), np.asarray(dst), np.asarray(edge_attr_3)
    src_pad = np.zeros(EP, src.dtype)
    src_pad[:E] = src
    dst_ext = np.full(EP + 2, N, dst.dtype)
    dst_ext[0], dst_ext[1:E + 1], dst_ext[-1] = -1, dst, -2
    attr_t = np.zeros((3, EP), attr.dtype)
    attr_t[:, :E] = attr.T

    def cols(v):
        return np.ascontiguousarray(v.reshape(ET, P).T)

    index_cols = np.concatenate([cols(src_pad).reshape(P, EB, TB), cols(dst_ext[1:-1]).reshape(P, EB, TB)], axis=2)
    ins = {
        "x": x, "edge_index_cols": index_cols.reshape(P, -1), "edge_dst_cols": cols(dst_ext[1:-1]),
        "edge_next_cols": cols(dst_ext[2:]), "dst_ext": dst_ext, "edge_attr_t": attr_t,
        "W": L0_gnn_W, "att_src": L0_gnn_att_src, "att_dst": L0_gnn_att_dst, "bias_gat": L0_gnn_bias_gat,
        "gate_weights": L0_gnn_gate_weights, "gamma_cols": np.asarray(L0_gnn_ln_gamma).reshape(A, P).T,
        "beta_cols": np.asarray(L0_gnn_ln_beta).reshape(A, P).T, "Wo": L0_gnn_Wo, "bo": L0_gnn_bo,
        "W1": L1_gnn_W1, "b1": L1_gnn_b1, "W2": L1_gnn_W2, "b2": L1_gnn_b2, "Wc": L1_gnn_Wc, "bc": L1_gnn_bc,
    }
    nc = _bacc.Bacc("TRN2", target_bir_lowering=False, num_devices=1)
    arrays, args = {}, {}
    for name, value in ins.items():
        value = np.ascontiguousarray(value)
        arrays[f"in_{name}"] = value
        args[name] = nc.dram_tensor(f"in_{name}", value.shape, mybir.dt.from_np(value.dtype), kind="ExternalInput").ap()
    args["out"] = nc.dram_tensor("out_x", (N, D), FP32, kind="ExternalOutput").ap()
    build(nc, **args)
    return _run(nc, [arrays], core_ids=[0]).results[0]["out_x"]
```
